# Optimizing a Trainium2 kernel written in Bass

```python
import numpy as np
import jax
import jax.numpy as jnp

def _softmax(x, axis=-1):
    return jax.nn.softmax(x, axis=axis)

def _gelu(x):
    return jax.nn.gelu(x, approximate=True)

def _silu(x):
    return jax.nn.silu(x)

def _sigmoid(x):
    return jax.nn.sigmoid(x)

def _layernorm(x, axis=-1, eps=1e-05):
    m = jnp.mean(x, axis=axis, keepdims=True)
    v = jnp.var(x, axis=axis, keepdims=True)
    return (x - m) / jnp.sqrt(v + eps)

def _scatter_add(tgt, idx, src, axis=0):
    return tgt.at[idx].add(src)

def _segment_sum(src, seg, n):
    return jax.ops.segment_sum(src, seg, n)
kernel_name = 'mk_flamingo_gated_d1_seqx_r2_9d30e7'

def setup_inputs(seed: int=0):
    np.random.seed(seed)
    _w = jnp.asarray

    def _rec_inputs():
        import jax
        import jax.numpy as jnp
        _rk = jax.random.key(seed)
        x = 0.5 + 0.2887 * jax.random.normal(jax.random.fold_in(_rk, 1), (4, 1024, 1024), jnp.float32)
        _lenS = 1024 - jax.random.randint(jax.random.fold_in(_rk, 7), (4,), 0, max(1, 1024 // 4) + 1, jnp.int32)
        _lenS2 = 1024 - jax.random.randint(jax.random.fold_in(_rk, 8), (4,), 0, max(1, 1024 // 4) + 1, jnp.int32)
        _ctx_512P = jax.random.normal(jax.random.fold_in(_rk, 11), (4, 16, 256), jnp.float32)
        _ctx_512c = jax.random.dirichlet(jax.random.fold_in(_rk, 511), 0.3 * jnp.ones((16,), jnp.float32), (4, 1024))
        _ctx_512t = jnp.einsum('bsk,bkd->bsd', _ctx_512c, _ctx_512P)
        _ctx_512t = _ctx_512t * jax.lax.rsqrt(jnp.mean(jnp.square(_ctx_512t)) + 1e-12) * 0.953939
        ctx_512 = 7.22013e-05 + 1.00017 * (_ctx_512t + 0.3 * jax.random.normal(jax.random.fold_in(_rk, 611), (4, 1024, 256), jnp.float32))
        _g = jax.random.normal(jax.random.fold_in(_rk, 9001), (2, 1), jnp.float32)
        _g = jnp.sign(_g) * jnp.maximum(jnp.abs(_g), 1.0) + (_g == 0) * 1.0
        g_xattn = _g[0]
        g_ffn = _g[1]
        return (x, ctx_512, g_xattn, g_ffn)
    x, ctx_512, g_xattn, g_ffn = _rec_inputs()

    def _L0_xattn_setup():
        import jax, jax.numpy as jnp
        import numpy as np
        P_ASEM = 0.6
        key = jax.random.key(seed)
        k1, k2, k3 = jax.random.split(key, 3)
        B, N, D = (8, 1024, 256)
        x = jax.random.normal(k1, (B, N, D), dtype=jnp.float32)
        adj = jax.random.uniform(k2, (B, N, N), dtype=jnp.float32)
        bound = 1.0 / np.sqrt(2 * D)
        W = jax.random.uniform(k3, (1, 2 * D), dtype=jnp.float32, minval=-bound, maxval=bound)
        b = jnp.zeros((1,), dtype=jnp.float32)
        return {'x': x, 'adj': adj, 'W': W, 'b': b}
    _L0_xattn_all = _L0_xattn_setup()
    _L0_xattn_in = {k: v for k, v in _L0_xattn_all.items() if k in ('W', 'b')}
    del _L0_xattn_all

    def _L0_ffn_setup():
        import jax, jax.numpy as jnp
        import numpy as np
        B, S, H, E = (4, 1024, 1024, 8)
        key = jax.random.key(seed)
        k_x, k_wg, k_w, k_b = jax.random.split(key, 4)
        x = jax.random.normal(k_x, (B, S, H), dtype=jnp.float32)
        wg = jax.random.normal(k_wg, (H, E), dtype=jnp.float32) * (1.0 / np.sqrt(H))
        W = jax.random.normal(k_w, (E, H, H), dtype=jnp.float32) * (1.0 / np.sqrt(H))
        b = jax.random.normal(k_b, (E, H), dtype=jnp.float32) * 0.01
        return {'x': x, 'wg': wg, 'W': W, 'b': b}
    _L0_ffn_all = _L0_ffn_setup()
    _L0_ffn_in = {k: v for k, v in _L0_ffn_all.items() if k in ('wg', 'W', 'b')}
    del _L0_ffn_all
    return {'x': x, 'ctx_512': ctx_512, 'g_xattn': g_xattn, 'g_ffn': g_ffn, 'L0_xattn_W': _L0_xattn_in['W'], 'L0_xattn_b': _L0_xattn_in['b'], 'L0_ffn_wg': _L0_ffn_in['wg'], 'L0_ffn_W': _L0_ffn_in['W'], 'L0_ffn_b': _L0_ffn_in['b']}

def reference(x, ctx_512, g_xattn, g_ffn, L0_xattn_W, L0_xattn_b, L0_ffn_wg, L0_ffn_W, L0_ffn_b):
    import jax
    import jax.numpy as jnp

    def _L0_xattn_ref(x, adj, W, b):
        import jax, jax.numpy as jnp
        import numpy as np
        P_ASEM = 0.6
        D = x.shape[-1]
        Wi = W[:, :D]
        Wj = W[:, D:]
        si = jnp.einsum('bnd,d->bn', x, Wi[0])
        sj = jnp.einsum('bnd,d->bn', x, Wj[0])
        xij = jax.nn.sigmoid(si[:, :, None] + sj[:, None, :] + b[0])
        return P_ASEM * xij + (1.0 - P_ASEM) * adj

    def _L0_ffn_ref(x, wg, W, b):
        import jax, jax.numpy as jnp
        import numpy as np
        B, S, H, E = (4, 1024, 1024, 8)
        Bv, Sv, Hv = x.shape
        Ev = W.shape[0]
        xt = x.reshape(-1, Hv)
        logits = xt @ wg
        probs = jax.nn.softmax(logits, axis=-1)
        idx = jnp.argmax(probs, axis=-1)
        gate = jnp.take_along_axis(probs, idx[:, None], axis=1)
        onehot = jax.nn.one_hot(idx, Ev, dtype=x.dtype)
        expert_out = jnp.einsum('nh,eoh->neo', xt, W) + b[None, :, :]
        combine = onehot * gate
        out = jnp.einsum('ne,neo->no', combine, expert_out)
        return out.reshape(Bv, Sv, Hv)
    x = x + jnp.tanh(g_xattn[0]) * _L0_xattn_ref(ctx_512, _layernorm(x, axis=-1), L0_xattn_W, L0_xattn_b)
    x = x + jnp.tanh(g_ffn[0]) * _L0_ffn_ref(_layernorm(x, axis=-1), L0_ffn_wg, L0_ffn_W, L0_ffn_b)
    return x

_drawn_inputs = setup_inputs


def setup_inputs(seed=0):
    import zlib

    import numpy as np

    out = dict(_drawn_inputs(seed))
    spreads = {}
    factors = {'L0_ffn_b': 8.0}
    for name, (base, spread) in spreads.items():
        noise = np.random.default_rng([zlib.crc32(name.encode()), seed]).standard_normal(out[name].shape)
        drawn = base * np.exp(spread * noise) if base else spread * noise
        out[name] = jnp.asarray(drawn.astype(out[name].dtype))
    for name, factor in factors.items():
        out[name] = (out[name] * factor).astype(out[name].dtype)
    return out
```

```python
from contextlib import ExitStack

import numpy as np

import concourse.bass as bass
from concourse import mybir

P = 128
F32 = mybir.dt.float32
F32R = mybir.dt.float32r
U32 = mybir.dt.uint32
I32 = mybir.dt.int32
ALU = mybir.AluOpType
ACT = mybir.ActivationFunctionType
AX = mybir.AxisListType

MIX = 0.6
EPS = 1e-5


def build(nc, x, ctx, g_xattn, g_ffn, mix_w, mix_b, wg, W, bias, out):
    B, S, H = x.shape
    D = ctx.shape[2]
    E = W.shape[0]
    N = B * S
    T = N // P
    K = H // P
    DC = D // P
    TB = S // P
    RING = 4
    assert (K, TB, DC) == (8, 8, 2) and T % RING == 0
    SLOTS = (N + E * (P - 1)) // P + 1
    assert SLOTS % RING == 0
    TAB = SLOTS + RING
    HALF = 512
    KH = K // 2
    G = 2 * K
    WP = 4
    SJ_RING = 2 * TB
    NOBODY = 2 * N
    META = 4

    x_t = x.rearrange("b s h -> (b s) h").rearrange("(t p) h -> t p h", p=P)
    ctx_t = ctx.rearrange("b s d -> (b s) d").rearrange("(t p) d -> t p d", p=P)
    out_rows = out.rearrange("b s h -> (b s) h")
    x1_rows = nc.dram_tensor("x1_rows", [N, H], F32, kind="Internal").ap()
    x1_t = x1_rows.rearrange("(t p) h -> t p h", p=P)
    w_blocks = W.rearrange("e (j p) h -> e j p h", p=P)

    st = ExitStack()
    with st:
        def sb(name, shape, dt=F32, where=st):
            return where.enter_context(nc.sbuf_tensor(name, shape, dt))

        def sem(name):
            return st.enter_context(nc.semaphore(name))

        ident = sb("ident", [P, P])
        w_raw = sb("w_raw", [P, K, H])
        bias_bc = sb("bias_bc", [P, 2, H])
        slot_meta = sb("slot_meta", [P, META, TAB])
        slot_row = sb("slot_row", [P, TAB], U32)
        gather_row = sb("gather_row", [P, RING], U32)
        scatter_row = sb("scatter_row", [P, RING], U32)
        n_filled = sb("n_filled", [1, 1], I32)
        slot_tab = sb("slot_tab", [1, 2, TAB], I32)

        zone1 = ExitStack()
        with zone1:
            x_in = sb("x_in", [P, RING, H], F32, zone1)
            ctx_in = sb("ctx_in", [P, RING, D], F32, zone1)
            ctx_tr = sb("ctx_tr", [P, 2, DC, P], F32, zone1)
            x1_tr = sb("x1_tr", [P, K, P], F32, zone1)
            sj = sb("sj", [P, SJ_RING, P + 2], F32, zone1)
            zone1_end = nc.sbuf_base

        x_gat = sb("x_gat", [P, RING, H])
        xn = sb("xn", [P, H])
        xt_hi = sb("xt_hi", [P, K, P], F32R)
        xt_lo = sb("xt_lo", [P, K, P], F32R)
        res = sb("res", [P, 2, H])
        assert zone1_end <= nc.sbuf_base

        zone2 = ExitStack()
        with zone2:
            sb("even_weights", [P, 2, K, H], F32, zone2)
            tiles_zone = ExitStack()
            with tiles_zone:
                x1 = sb("x1", [P, RING, H], F32, tiles_zone)
                sig = sb("sig", [P, 2, H], F32, tiles_zone)
                lin = sb("lin", [P, 2, H], F32, tiles_zone)
                tiles_end = nc.sbuf_base
            slot_hot = sb("slot_hot", [P, T, TAB], F32, zone2)
            slot_val = sb("slot_val", [P, T, META, TAB], F32, zone2)
            sb("gap", [P, (tiles_end - nc.sbuf_base) // 4], F32, zone2)

            def sa(name, shape, dt=F32):
                return sb(name, shape, dt, zone2)

            lane_hot = sa("lane_hot", [P, T, P])
            ones = sa("ones", [P, P])
            before = sa("before", [P, P])
            wcol = sa("wcol", [P, 2 * DC])
            wj_bc = sa("wj_bc", [P, DC, P])
            gates = sa("gates", [P, 3])
            th = sa("th", [P, 2])
            c_sig = sa("c_sig", [P, 1])
            c_ln = sa("c_ln", [P, 1])
            half_b = sa("half_b", [P, 1])
            minus_half = sa("minus_half", [P, T])
            wg_sb = sa("wg_sb", [P, K, E])
            wg_mean = sa("wg_mean", [P, E])
            wg_c = sa("wg_c", [P, K, E])
            ln_raw = sa("ln_raw", [P, 2, 2, 6])
            ln_mv = sa("ln_mv", [P, 2, 2])
            ln_rs = sa("ln_rs", [P, 2, 4])
            ln_b = sa("ln_b", [P, 2])
            x1_raw = sa("x1_raw", [P, 2, 2, 6])
            mv_ring = sa("mv_ring", [P, RING, 2])
            x1_mv = sa("x1_mv", [P, T, 2])
            iota_lane = sa("iota_lane", [P, P])
            iota_slot = sa("iota_slot", [P, TAB])
            iota_full = sa("iota_full", [P, T])
            iota_pick = sa("iota_pick", [P, E])
            lg = sa("lg", [P, T, E])
            onehot = sa("onehot", [P, T, E])
            r1 = sa("r1", [P, T, E])
            r2 = sa("r2", [P, E, T])
            r3 = sa("r3", [P, E, T])
            seg = sa("seg", [P, E, T])
            t1 = sa("t1", [P, T])
            t2 = sa("t2", [P, T])
            off_f = sa("off_f", [P, T])
            off_i = sa("off_i", [P, T], I32)
            quo_i = sa("quo_i", [P, T], I32)
            lane_i = sa("lane_i", [P, T], I32)
            lane = sa("lane", [P, T])
            slot = sa("slot", [P, T])
            meta = sa("meta", [P, META, T])
            n_slots = sa("n_slots", [P, E])
            slot_end = sa("slot_end", [P, E])
            slot_start = sa("slot_start", [P, E])
            cmp_a = sa("cmp_a", [1, TAB, E])
            cmp_b = sa("cmp_b", [1, TAB, E])
            tab_f = sa("tab_f", [1, 4, TAB])
            zone2_end = nc.sbuf_base
        wt = sb("wt", [P, 2, 2, K, H], F32R)
        assert zone2_end <= nc.sbuf_base

        bank = [st.enter_context(nc.psum_tensor(f"bank{i}", [P, HALF], F32)) for i in range(8)]
        out_ps = bank[0:2]
        xt_ps = bank[2:4]
        w_ps = bank[4:8]
        ctx_ps, sj_ps, lg_ps = bank[4], bank[5], bank[6]
        mean_ps, rank_ps, total_ps, meta_ps = bank[7], bank[0], bank[1], bank[7]

        x_landed = [sem(f"x_landed{r}") for r in range(RING)]
        ctx_landed = [sem(f"ctx_landed{r}") for r in range(RING)]
        x1_stored = [sem(f"x1_stored{r}") for r in range(RING)]
        w_landed = [sem(f"w_landed{j}") for j in range(K)]
        row_landed = [sem(f"row_landed{r}") for r in range(RING)]
        row_stored = [sem(f"row_stored{r}") for r in range(2)]
        gates_landed = sem("gates_landed")
        wcol_landed = sem("wcol_landed")
        wg_landed = sem("wg_landed")
        bias_landed = sem("bias_landed")
        pool_step = sem("pool_step")
        dve_step = sem("dve_step")
        pool_passed = sem("pool_passed")
        dve_passed = sem("dve_passed")
        masks_ready = sem("masks_ready")
        tanh_ready = sem("tanh_ready")
        scales_ready = sem("scales_ready")
        wj_ready = sem("wj_ready")
        mean_ready = sem("mean_ready")
        wgc_ready = sem("wgc_ready")
        ctx_turned = sem("ctx_turned")
        ctx_copied = sem("ctx_copied")
        sj_summed = sem("sj_summed")
        sj_ready = sem("sj_ready")
        sig_ready = sem("sig_ready")
        raw_ready = sem("raw_ready")
        mv_ready = sem("mv_ready")
        lin_ready = sem("lin_ready")
        x1_ready = sem("x1_ready")
        raw1_ready = sem("raw1_ready")
        mv1_ready = sem("mv1_ready")
        mv_kept = sem("mv_kept")
        x1_turned = sem("x1_turned")
        x1_copied = sem("x1_copied")
        logits_ready = sem("logits_ready")
        lgmax_ready = sem("lgmax_ready")
        exp_ready = sem("exp_ready")
        rstd_in = sem("rstd_in")
        rstd_ready = sem("rstd_ready")
        iotas_ready = sem("iotas_ready")
        onehot_ready = sem("onehot_ready")
        ranks_ready = sem("ranks_ready")
        hot_ready = sem("hot_ready")
        meta_ready = sem("meta_ready")
        route_ready = sem("route_ready")
        w_turned = sem("w_turned")
        w_hi_ready = sem("w_hi_ready")
        w_lo_ready = sem("w_lo_ready")
        xn_ready = sem("xn_ready")
        xt_turned = [sem(f"xt_turned{g}") for g in range(2)]
        xt_hi_ready = [sem(f"xt_hi_ready{g}") for g in range(2)]
        xt_ready = [sem(f"xt_ready{g}") for g in range(2)]
        xt_used = sem("xt_used")
        sum_ready = [sem(f"sum_ready{h}") for h in range(2)]
        biased = sem("biased")
        res_ready = [sem(f"res_ready{h}") for h in range(2)]

        block = st.enter_context(nc.Block())

        MAIN = (T - TB) // RING
        LAST = T // RING - 1

        @block.sync
        def _(sp):
            sp.dma_start(gates[:, 0:1], g_xattn.unsqueeze(0).to_broadcast([P, 1])).then_inc(gates_landed, 16)
            sp.dma_start(gates[:, 1:2], g_ffn.unsqueeze(0).to_broadcast([P, 1])).then_inc(gates_landed, 16)
            sp.dma_start(gates[:, 2:3], mix_b.unsqueeze(0).to_broadcast([P, 1])).then_inc(gates_landed, 16)
            with nc.allow_non_contiguous_dma(reason="512 weights, once, as columns"):
                sp.dma_start(wcol[:, :], mix_w.rearrange("a (c p) -> p (a c)", p=P)).then_inc(wcol_landed, 16)
            for c in range(RING):
                sp.dma_start(ctx_in[:, c, :], ctx_t[c]).then_inc(ctx_landed[c], 16)
            sp.dma_start(wg_sb[:, :, :], wg.rearrange("(k p) e -> p k e", p=P)).then_inc(wg_landed, 16)
            for r in range(RING):
                sp.dma_start(x_in[:, r, :], x_t[r]).then_inc(x_landed[r], 16)
            for c in range(RING, TB):
                sp.wait_ge(ctx_turned, c - RING + 1)
                sp.dma_start(ctx_in[:, c % RING, :], ctx_t[c]).then_inc(ctx_landed[c % RING], 16)

            def tiles(i, more_ctx, more_x):
                for r in range(RING):
                    t = RING * i + r
                    if more_x:
                        sp.wait_ge(lin_ready, t + 1)
                        sp.dma_start(x_in[:, r, :], x_t[t + RING]).then_inc(x_landed[r], 16)
                    if more_ctx:
                        sp.wait_ge(ctx_turned, t + RING + 1)
                        sp.dma_start(ctx_in[:, r, :], ctx_t[t + TB]).then_inc(ctx_landed[r], 16)
                    sp.wait_ge(x1_ready, t + 1)
                    sp.dma_start(x1_t[t], x1[:, r, :]).then_inc(x1_stored[r], 16)

            with sp.Fori(0, MAIN) as i:
                tiles(i, True, True)
            for i in range(MAIN, LAST):
                tiles(i, False, True)
            for j in range(K):
                sp.dma_start(w_raw[:, j, :], w_blocks[0, j]).then_inc(w_landed[j], 16)
            sp.dma_start(bias_bc[:, 0, :], bias[0:1, :].to_broadcast([P, H])).then_inc(bias_landed, 16)
            tiles(LAST, False, False)

            def load_weights(e):
                for j in range(K):
                    sp.wait_ge(w_turned, G * (e - 1) + 2 * j + 2)
                    sp.dma_start(w_raw[:, j, :], w_blocks[e, j]).then_inc(w_landed[j], 16)

            def load_bias(e):
                sp.wait_ge(w_lo_ready, G * e + 1)
                sp.dma_start(bias_bc[:, bass.ds(e % 2, 1), :].rearrange("p a h -> p (a h)"),
                             bias[bass.ds(e, 1), :].to_broadcast([P, H])).then_inc(bias_landed, 16)

            load_weights(1)
            with sp.Fori(1, E - 1) as e:
                load_bias(e)
                load_weights(e + 1)
            load_bias(E - 1)

        @block.gpsimd
        def _(pool):
            steps = [0]

            def link(ins):
                steps[0] += 1
                ins.then_inc(pool_step, 1)
                pool.wait_ge(pool_step, steps[0])

            nc.gpsimd.memset(minus_half[:, :], -0.5)
            link(nc.gpsimd.memset(ident[:, :], 0.0))
            link(nc.gpsimd.memset(ones[:, :], 1.0))
            link(nc.gpsimd.affine_select(out=ident[:, :], in_=ident[:, :], compare_op=ALU.not_equal, fill=1.0,
                                         base=0, pattern=[[-1, P]], channel_multiplier=1))
            nc.gpsimd.affine_select(out=before[:, :], in_=ones[:, :], compare_op=ALU.is_gt, fill=0.0,
                                    base=0, pattern=[[1, P]], channel_multiplier=-1).then_inc(masks_ready, 1)
            pool.wait_ge(scales_ready, 1)

            def settled(done, value):
                pool.wait_ge(done, value)
                pool.sem_inc(pool_passed, 1)

            def linear(t, r):
                p = r % 2
                first = steps[0] + 5 * t
                settled(mv_ready, t + 1)
                nc.gpsimd.tensor_scalar(ln_rs[:, p, 0:1], ln_mv[:, p, 1:2], EPS, None, ALU.add).then_inc(pool_step, 1)
                settled(pool_step, first + 1)
                nc.gpsimd.tensor_tensor(ln_rs[:, p, 1:2], ln_rs[:, p, 0:1], minus_half[:, 0:1],
                                        ALU.pow).then_inc(pool_step, 1)
                settled(pool_step, first + 2)
                nc.gpsimd.tensor_scalar(ln_rs[:, p, 2:3], ln_rs[:, p, 1:2], c_ln[:, 0:1], None,
                                        ALU.mult).then_inc(pool_step, 1)
                settled(pool_step, first + 3)
                nc.gpsimd.tensor_scalar(ln_rs[:, p, 3:4], ln_rs[:, p, 2:3], 1.0, None, ALU.add).then_inc(pool_step, 1)
                nc.gpsimd.tensor_scalar(ln_b[:, p:p + 1], ln_mv[:, p, 0:1], ln_rs[:, p, 2:3], -1.0,
                                        ALU.mult, ALU.mult).then_inc(pool_step, 1)
                settled(pool_step, first + 5)
                settled(x_landed[r], 16 * ((t - r) // RING + 1))
                nc.gpsimd.tensor_scalar(lin[:, p, :], x_in[:, r, :], ln_rs[:, p, 3:4], ln_b[:, p:p + 1],
                                        ALU.mult, ALU.add).then_inc(lin_ready, 1)

            def tiles(i, last=False):
                for r in range(RING):
                    t = RING * i + r
                    if last and r == RING - 1:
                        break
                    pool.wait_ge(x1_ready, t)
                    linear(t + 1, (r + 1) % RING)

            linear(0, 0)
            with pool.Fori(0, LAST) as i:
                tiles(i)
            tiles(LAST, last=True)
            steps[0] += 5 * T

            pool.wait_ge(rstd_in, 1)
            nc.gpsimd.tensor_tensor(meta[:, 2, :], t1[:, :], minus_half[:, :], ALU.pow).then_inc(rstd_ready, 1)
            nc.gpsimd.iota(iota_lane[:, :], [[1, P]], base=0, channel_multiplier=0,
                           allow_small_or_imprecise_dtypes=True)
            nc.gpsimd.iota(iota_slot[:, :], [[1, TAB]], base=0, channel_multiplier=0,
                           allow_small_or_imprecise_dtypes=True)
            nc.gpsimd.iota(iota_full[:, :], [[P, T]], base=0, channel_multiplier=0,
                           allow_small_or_imprecise_dtypes=True)
            nc.gpsimd.iota(iota_pick[:, :], [[-1, E]], base=E, channel_multiplier=0,
                           allow_small_or_imprecise_dtypes=True)
            nc.gpsimd.iota(meta[:, 0, :], [[P, T]], base=-NOBODY, channel_multiplier=1,
                           allow_small_or_imprecise_dtypes=True).then_inc(iotas_ready, 1)
            pool.wait_ge(exp_ready, 1)
            nc.gpsimd.memset(x_gat[:, :, :], 0.0)

            pool.wait_ge(route_ready, 1)
            for r in range(RING):
                pool.wait_ge(x1_stored[r], 16 * (T // RING))

            base = steps[0]

            def gather(t, r, nth):
                nc.gpsimd.tensor_copy(gather_row[:, r:r + 1], slot_row[:, bass.ds(t, 1)]).then_inc(pool_step, 1)
                settled(pool_step, base + nth + 1)
                nc.gpsimd.indirect_dma_start(
                    out=x_gat[:, r, :], out_offset=None, in_=x1_rows,
                    in_offset=bass.IndirectOffsetOnAxis(ap=gather_row[:, r:r + 1], axis=0),
                    bounds_check=N - 1, oob_is_err=False).then_inc(row_landed[r], 16)

            def scatter(t, r, nth):
                nc.gpsimd.tensor_copy(scatter_row[:, r:r + 1], slot_row[:, bass.ds(t, 1)]).then_inc(pool_step, 1)
                settled(pool_step, base + nth + 1)
                nc.gpsimd.indirect_dma_start(
                    out=out_rows, out_offset=bass.IndirectOffsetOnAxis(ap=scatter_row[:, r:r + 1], axis=0),
                    in_=res[:, r % 2, :], in_offset=None,
                    bounds_check=N - 1, oob_is_err=False).then_inc(row_stored[r % 2], 16)

            AHEAD = RING - 1
            for r in range(AHEAD):
                gather(r, r, r)
            with pool.Fori(0, SLOTS // RING) as i:
                for r in range(RING):
                    t = RING * i + r
                    kind = pool.value_load(slot_tab[0:1, 0, bass.ds(t, 1)], min_val=0, max_val=2)
                    with pool.If(kind > 0):
                        settled(res_ready[1], t)
                        gather(t + AHEAD, (r + AHEAD) % RING, AHEAD + 2 * t)
                        pool.wait_ge(res_ready[0], t + 1)
                        settled(res_ready[1], t + 1)
                        scatter(t, r, AHEAD + 2 * t + 1)
                    with pool.Else():
                        pool.nop()
            filled = pool.value_load(n_filled[0:1, 0:1], min_val=E, max_val=SLOTS - 1)
            for p in range(2):
                pool.wait_ge(row_stored[p], 16 * ((filled + 1 - p) // 2))

        @block.scalar
        def _(act):
            act.wait_ge(gates_landed, 48)
            nc.scalar.activation(th[:, :], gates[:, 0:2], ACT.Tanh).then_inc(tanh_ready, 1)

            def ctx_copy(c, r):
                act.wait_ge(ctx_turned, c + 1)
                nc.scalar.activation(ctx_tr[:, r % 2, :, :].rearrange("p c n -> p (c n)"), ctx_ps[:, 0:D],
                                     ACT.Copy).then_inc(ctx_copied, 1)

            def sj_copy(c):
                act.wait_ge(sj_summed, c + 1)
                nc.scalar.activation(sj[:, bass.ds(c % SJ_RING, 1), 0:P + 1].rearrange("p a n -> p (a n)"),
                                     sj_ps[:, 0:P + 1], ACT.Identity, bias=half_b[:, 0:1]).then_inc(sj_ready, 1)

            def sigmoid(t, r):
                act.wait_ge(sj_ready, TB * (t // TB) + TB)
                nc.scalar.activation(
                    sig[:, r % 2, :].rearrange("p (c n) -> p c n", n=P),
                    sj[:, bass.ds(TB * ((t // TB) % 2), TB), 0:P], ACT.Sigmoid,
                    bias=sj[:, bass.ds(t % SJ_RING, 1), P:P + 1].rearrange("p a n -> p (a n)")).then_inc(sig_ready, 1)

            act.wait_ge(scales_ready, 1)
            with act.Fori(0, TB // RING) as i:
                for r in range(RING):
                    ctx_copy(RING * i + r, r)
                    sj_copy(RING * i + r)
            sigmoid(0, 0)

            def tiles(i, more_ctx, last=False):
                for r in range(RING):
                    t = RING * i + r
                    if more_ctx:
                        ctx_copy(t + TB, r)
                    if more_ctx and r == RING - 1:
                        sj_copy(t + TB)
                    if not (last and r == RING - 1):
                        act.wait_ge(x1_ready, t)
                        sigmoid(t + 1, (r + 1) % RING)
                    if more_ctx and r < RING - 1:
                        sj_copy(t + TB)
                    for g in range(2):
                        act.wait_ge(x1_turned, 2 * t + g + 1)
                        nc.scalar.activation(x1_tr[:, KH * g:KH * (g + 1), :].rearrange("p k n -> p (k n)"),
                                             xt_ps[g][:, :], ACT.Copy).then_inc(x1_copied, 1)

            with act.Fori(0, MAIN) as i:
                tiles(i, True)
            for i in range(MAIN, LAST):
                tiles(i, False)
            tiles(LAST, False, last=True)

            act.wait_ge(lgmax_ready, 1)
            nc.scalar.activation(r1[:, :, :], r1[:, :, :], ACT.Exp).then_inc(exp_ready, 1)

            def cut_high(e, g, par):
                act.wait_ge(w_turned, G * e + g + 1)
                j, kh = g // 2, g % 2
                nc.scalar.activation(
                    wt[:, bass.ds(par, 1), 0, KH * kh:KH * (kh + 1), P * j:P * (j + 1)]
                    .rearrange("p a k o -> p (a k) o"),
                    w_ps[g % WP][:, :].rearrange("p (k o) -> p k o", k=KH), ACT.Copy).then_inc(w_hi_ready, 1)

            def normalise(t, r):
                act.wait_ge(row_landed[r], 16 * ((t - r) // RING + 1))
                nc.scalar.activation(xn[:, :], x_gat[:, r, :], ACT.Identity,
                                     bias=slot_meta[:, 3, bass.ds(t, 1)],
                                     scale=slot_meta[:, 2, bass.ds(t, 1)]).then_inc(xn_ready, 1)

            def xt_high(t, g, first=False):
                act.wait_ge(xt_turned[g], t + 1)
                if not first:
                    act.wait_ge(xt_used if g == 0 else sum_ready[1], t)
                nc.scalar.activation(xt_hi[:, KH * g:KH * (g + 1), :].rearrange("p k n -> p (k n)"),
                                     xt_ps[g][:, :], ACT.Copy).then_inc(xt_hi_ready[g], 1)

            for g in range(G):
                cut_high(0, g, 0)
            act.wait_ge(route_ready, 1)
            normalise(0, 0)
            for g in range(2):
                xt_high(0, g, first=True)
            with act.Fori(0, SLOTS // RING) as i:
                for r in range(RING):
                    t = RING * i + r
                    kind = act.value_load(slot_tab[0:1, 0, bass.ds(t, 1)], min_val=0, max_val=2)
                    with act.If(kind > 1):
                        e = act.value_load(slot_tab[0:1, 1, bass.ds(t, 1)], min_val=0, max_val=E - 1)
                        par = act.snap((e + 1) % 2)
                        normalise(t + 1, (r + 1) % RING)
                        for g in range(12):
                            cut_high(e + 1, g, par)
                        xt_high(t + 1, 0)
                        for g in range(12, G):
                            cut_high(e + 1, g, par)
                        xt_high(t + 1, 1)
                    with act.Else():
                        with act.If(kind > 0):
                            normalise(t + 1, (r + 1) % RING)
                            for g in range(2):
                                xt_high(t + 1, g)
                        with act.Else():
                            act.nop()
                        act.nop()

        @block.vector
        def _(dve):
            steps = [0]

            def link(ins):
                steps[0] += 1
                ins.then_inc(dve_step, 1)
                dve.wait_ge(dve_step, steps[0])

            dve.wait_ge(tanh_ready, 1)
            nc.vector.tensor_scalar(c_sig[:, :], th[:, 0:1], MIX, None, ALU.mult)
            nc.vector.tensor_scalar(c_ln[:, :], th[:, 0:1], 1.0 - MIX, None, ALU.mult)
            nc.vector.tensor_scalar(half_b[:, :], gates[:, 2:3], 0.5, None, ALU.mult).then_inc(scales_ready, 1)
            dve.wait_ge(wcol_landed, 16)
            for c in range(DC):
                last = nc.vector.tensor_copy(wj_bc[:, c, :], wcol[:, DC + c:DC + c + 1].to_broadcast([P, P]))
            last.then_inc(wj_ready, 1)
            dve.wait_ge(mean_ready, 1)
            link(nc.vector.tensor_reduce(wg_mean[:, :], mean_ps[:, 0:K * E].rearrange("p (k e) -> p e k", k=K),
                                         AX.X, ALU.add))
            link(nc.vector.tensor_scalar(wg_mean[:, :], wg_mean[:, :], 1.0 / H, None, ALU.mult))
            nc.vector.tensor_tensor(wg_c[:, :, :], wg_sb[:, :, :],
                                    wg_mean[:, :].unsqueeze(1).to_broadcast([P, K, E]),
                                    ALU.subtract).then_inc(wgc_ready, 1)

            def settled(done, value):
                dve.wait_ge(done, value)
                dve.sem_inc(dve_passed, 1)

            def stats(t, r):
                p = r % 2
                dve.wait_ge(x_landed[r], 16 * ((t - r) // RING + 1))
                nc.vector.bn_stats(ln_raw[:, p, 0, :], x_in[:, r, 0:HALF])
                nc.vector.bn_stats(ln_raw[:, p, 1, :], x_in[:, r, HALF:H]).then_inc(raw_ready, 1)
                settled(raw_ready, t + 1)
                nc.vector.bn_aggr(ln_mv[:, p, :], ln_raw[:, p, :, :].rearrange("p a b -> p (a b)")).then_inc(mv_ready, 1)

            def mix(t, r):
                p = r % 2
                dve.wait_ge(sig_ready, t + 1)
                dve.wait_ge(lin_ready, t + 1)
                dve.wait_ge(x1_stored[r], 16 * ((t - r) // RING))
                nc.vector.scalar_tensor_tensor(out=x1[:, r, :], in0=sig[:, p, :], scalar=c_sig[:, 0:1],
                                               in1=lin[:, p, :], op0=ALU.mult, op1=ALU.add).then_inc(x1_ready, 1)
                dve.wait_ge(x1_ready, t + 1)
                nc.vector.bn_stats(x1_raw[:, p, 0, :], x1[:, r, 0:HALF])
                nc.vector.bn_stats(x1_raw[:, p, 1, :], x1[:, r, HALF:H]).then_inc(raw1_ready, 1)
                settled(raw1_ready, t + 1)
                nc.vector.bn_aggr(mv_ring[:, r, :], x1_raw[:, p, :, :].rearrange("p a b -> p (a b)")).then_inc(mv1_ready, 1)

            def tiles(i, last=False):
                for r in range(RING):
                    t = RING * i + r
                    if not (last and r == RING - 1):
                        dve.wait_ge(lin_ready, t)
                        stats(t + 1, (r + 1) % RING)
                    mix(t, r)
                dve.wait_ge(mv1_ready, RING * i + RING)
                nc.vector.tensor_copy(x1_mv[:, bass.ds(RING * i, RING), :], mv_ring[:, :, :]).then_inc(mv_kept, 1)

            stats(0, 0)
            with dve.Fori(0, LAST) as i:
                tiles(i)
            tiles(LAST, last=True)

            dve.wait_ge(mv_kept, T // RING)
            link(nc.vector.tensor_scalar(t1[:, :], x1_mv[:, :, 1], EPS, None, ALU.add))
            nc.vector.engine_nop().then_inc(rstd_in, 1)
            dve.wait_ge(rstd_ready, 1)
            link(nc.vector.scalar_tensor_tensor(out=meta[:, 3, :], in0=x1_mv[:, :, 0], scalar=-1.0,
                                                in1=meta[:, 2, :], op0=ALU.mult, op1=ALU.mult))
            dve.wait_ge(logits_ready, T)
            link(nc.vector.tensor_tensor(lg[:, :, :], lg_ps[:, 0:T * E].rearrange("p (t e) -> p t e", e=E),
                                         meta[:, 2, :].unsqueeze(2).to_broadcast([P, T, E]), ALU.mult))
            link(nc.vector.reduce_max(t2[:, :], lg[:, :, :], AX.X))
            nc.vector.tensor_tensor(r1[:, :, :], lg[:, :, :], t2[:, :].unsqueeze(2).to_broadcast([P, T, E]),
                                    ALU.subtract).then_inc(lgmax_ready, 1)
            link(nc.vector.tensor_tensor(onehot[:, :, :], lg[:, :, :],
                                         t2[:, :].unsqueeze(2).to_broadcast([P, T, E]), ALU.is_equal))
            dve.wait_ge(iotas_ready, 1)
            link(nc.vector.tensor_tensor(onehot[:, :, :], onehot[:, :, :],
                                         iota_pick[:, :].unsqueeze(1).to_broadcast([P, T, E]), ALU.mult))
            link(nc.vector.reduce_max(t2[:, :], onehot[:, :, :], AX.X))
            link(nc.vector.tensor_tensor(onehot[:, :, :], onehot[:, :, :],
                                         t2[:, :].unsqueeze(2).to_broadcast([P, T, E]), ALU.is_equal))
            nc.vector.engine_nop().then_inc(onehot_ready, 1)
            dve.wait_ge(exp_ready, 1)
            link(nc.vector.reduce_sum(t1[:, :], r1[:, :, :], AX.X))
            link(nc.vector.reciprocal(t1[:, :], t1[:, :]))
            link(nc.vector.tensor_scalar(meta[:, 1, :], t1[:, :], th[:, 1:2], None, ALU.mult))
            link(nc.vector.memset(seg[:, :, :], 1.0))
            link(nc.vector.memset(seg[:, :, 0:1], 0.0))
            dve.wait_ge(ranks_ready, 1)
            totals = total_ps[:, 0:T * E].rearrange("p (t e) -> p e t", e=E)
            link(nc.vector.tensor_copy(r3[:, :, :], totals))
            link(nc.vector.tensor_tensor_scan(r2[:, :, :].rearrange("p e t -> p (e t)"),
                                              seg[:, :, :].rearrange("p e t -> p (e t)"),
                                              r3[:, :, :].rearrange("p e t -> p (e t)"), 0.0, ALU.mult, ALU.add))
            link(nc.vector.tensor_tensor(seg[:, :, :], r2[:, :, T - 1:T].to_broadcast([P, E, T]),
                                         iota_full[:, :].unsqueeze(1).to_broadcast([P, E, T]), ALU.is_gt))
            link(nc.vector.reduce_sum(n_slots[:, :], seg[:, :, :], AX.X))
            link(nc.vector.tensor_scalar(n_slots[:, :], n_slots[:, :], 1.0, None, ALU.max))
            link(nc.vector.tensor_tensor_scan(slot_end[:, :], ones[:, 0:E], n_slots[:, :], 0.0, ALU.mult, ALU.add))
            link(nc.vector.tensor_tensor(slot_start[:, :], slot_end[:, :], n_slots[:, :], ALU.subtract))
            link(nc.vector.tensor_tensor(r2[:, :, :], r2[:, :, :], r3[:, :, :], ALU.subtract))
            link(nc.vector.tensor_tensor(r1[:, :, :], r2[:, :, :].rearrange("p e t -> p t e"),
                                         rank_ps[:, 0:T * E].rearrange("p (t e) -> p t e", e=E), ALU.add))
            link(nc.vector.tensor_tensor(r1[:, :, :], r1[:, :, :], onehot[:, :, :], ALU.mult))
            link(nc.vector.reduce_sum(off_f[:, :], r1[:, :, :], AX.X))
            link(nc.vector.tensor_tensor(r1[:, :, :], onehot[:, :, :],
                                         slot_start[:, :].unsqueeze(1).to_broadcast([P, T, E]), ALU.mult))
            link(nc.vector.reduce_sum(t2[:, :], r1[:, :, :], AX.X))
            link(nc.vector.tensor_copy(off_i[:, :], off_f[:, :]))
            link(nc.vector.tensor_scalar(quo_i[:, :], off_i[:, :], 7, None, ALU.arith_shift_right))
            link(nc.vector.tensor_scalar(lane_i[:, :], off_i[:, :], P - 1, None, ALU.bitwise_and))
            link(nc.vector.tensor_copy(lane[:, :], lane_i[:, :]))
            link(nc.vector.tensor_copy(off_f[:, :], quo_i[:, :]))
            link(nc.vector.tensor_tensor(slot[:, :], off_f[:, :], t2[:, :], ALU.add))
            for r in range(RING):
                dve.wait_ge(x1_stored[r], 16 * (T // RING))
            link(nc.vector.tensor_tensor(slot_hot[:, :, :], iota_slot[:, :].unsqueeze(1).to_broadcast([P, T, TAB]),
                                         slot[:, :].unsqueeze(2).to_broadcast([P, T, TAB]), ALU.is_equal))
            nc.vector.tensor_tensor(lane_hot[:, :, :], iota_lane[:, :].unsqueeze(1).to_broadcast([P, T, P]),
                                    lane[:, :].unsqueeze(2).to_broadcast([P, T, P]), ALU.is_equal)
            for m in range(META):
                last = nc.vector.tensor_tensor(slot_val[:, :, m, :], slot_hot[:, :, :],
                                               meta[:, m, :].unsqueeze(2).to_broadcast([P, T, TAB]), ALU.mult)
            last.then_inc(hot_ready, 1)
            slots_all = iota_slot[0:1, :].unsqueeze(2).to_broadcast([1, TAB, E])
            starts = slot_start[0:1, :].unsqueeze(1).to_broadcast([1, TAB, E])
            link(nc.vector.tensor_tensor(cmp_a[:, :, :], slots_all, starts, ALU.is_ge))
            link(nc.vector.reduce_sum(tab_f[:, 0, :], cmp_a[:, :, :], AX.X))
            link(nc.vector.tensor_tensor(cmp_b[:, :, :], slots_all, starts, ALU.is_equal))
            link(nc.vector.reduce_sum(tab_f[:, 1, :], cmp_b[:, :, 0:E - 1], AX.X))
            link(nc.vector.tensor_tensor(tab_f[:, 2, :], iota_slot[0:1, :],
                                         slot_end[0:1, E - 1:E].to_broadcast([1, TAB]), ALU.is_lt))
            link(nc.vector.tensor_tensor(tab_f[:, 3, :], tab_f[:, 1, :], tab_f[:, 2, :], ALU.add))
            link(nc.vector.tensor_copy(slot_tab[:, 0, :], tab_f[:, 3, :]))
            link(nc.vector.tensor_copy(n_filled[:, :], slot_end[0:1, E - 1:E]))
            link(nc.vector.tensor_scalar(tab_f[:, 0, :], tab_f[:, 0, :], -1.0, None, ALU.add))
            link(nc.vector.tensor_copy(slot_tab[:, 1, :], tab_f[:, 0, :]))
            dve.wait_ge(meta_ready, 1)
            link(nc.vector.tensor_copy(slot_meta[:, :, :].rearrange("p m s -> p (m s)"), meta_ps[:, 0:META * TAB]))
            link(nc.vector.tensor_scalar(slot_row[:, :], slot_meta[:, 0, :], float(NOBODY), None, ALU.add))
            nc.vector.engine_nop().then_inc(route_ready, 1)

            def cut_low(e, g, par):
                dve.wait_ge(w_hi_ready, G * e + g + 1)
                j, kh = g // 2, g % 2
                where = wt[:, bass.ds(par, 1), :, KH * kh:KH * (kh + 1), P * j:P * (j + 1)]
                nc.vector.tensor_tensor(where[:, :, 1].rearrange("p a k o -> p (a k) o"),
                                        w_ps[g % WP][:, :].rearrange("p (k o) -> p k o", k=KH),
                                        where[:, :, 0].rearrange("p a k o -> p (a k) o").bitcast(F32),
                                        ALU.subtract).then_inc(w_lo_ready, 1)

            def xt_low(t, g):
                dve.wait_ge(xt_hi_ready[g], t + 1)
                nc.vector.tensor_tensor(xt_lo[:, KH * g:KH * (g + 1), :].rearrange("p k n -> p (k n)"),
                                        xt_ps[g][:, :],
                                        xt_hi[:, KH * g:KH * (g + 1), :].rearrange("p k n -> p (k n)").bitcast(F32),
                                        ALU.subtract).then_inc(xt_ready[g], 1)

            def finish(i, r, t, h, par):
                cols = slice(HALF * h, HALF * (h + 1))
                if h == 0:
                    dve.wait_ge(row_stored[r % 2], 32 * i + 16 * (r // 2))
                dve.wait_ge(sum_ready[h], t + 1)
                nc.vector.tensor_tensor(res[:, r % 2, cols], out_ps[h][:, :],
                                        bias_bc[:, bass.ds(par, 1), cols].rearrange("p a o -> p (a o)"),
                                        ALU.add).then_inc(biased, 1)
                dve.wait_ge(biased, 2 * t + h + 1)
                nc.vector.scalar_tensor_tensor(out=res[:, r % 2, cols], in0=res[:, r % 2, cols],
                                               scalar=slot_meta[:, 1, bass.ds(t, 1)], in1=x_gat[:, r, cols],
                                               op0=ALU.mult, op1=ALU.add).then_inc(res_ready[h], 1)

            for g in range(G):
                cut_low(0, g, 0)
            for g in range(2):
                xt_low(0, g)
            with dve.Fori(0, SLOTS // RING) as i:
                for r in range(RING):
                    t = RING * i + r
                    kind = dve.value_load(slot_tab[0:1, 0, bass.ds(t, 1)], min_val=0, max_val=2)
                    e = dve.value_load(slot_tab[0:1, 1, bass.ds(t, 1)], min_val=0, max_val=E - 1)
                    par = dve.snap(e % 2)
                    with dve.If(kind > 1):
                        nxt = dve.snap((e + 1) % 2)
                        dve.wait_ge(bias_landed, 16 * e + 16)
                        for g in range(8):
                            cut_low(e + 1, g, nxt)
                        finish(i, r, t, 0, par)
                        for g in range(8, 12):
                            cut_low(e + 1, g, nxt)
                        xt_low(t + 1, 0)
                        for g in range(12, G):
                            cut_low(e + 1, g, nxt)
                        xt_low(t + 1, 1)
                        finish(i, r, t, 1, par)
                    with dve.Else():
                        with dve.If(kind > 0):
                            dve.wait_ge(bias_landed, 16 * e + 16)
                            finish(i, r, t, 0, par)
                            for g in range(2):
                                xt_low(t + 1, g)
                            finish(i, r, t, 1, par)
                        with dve.Else():
                            dve.nop()
                        dve.nop()

        @block.tensor
        def _(pe):
            pe.wait_ge(masks_ready, 1)
            pe.wait_ge(wg_landed, 16)
            nc.tensor.matmul(mean_ps[:, 0:K * E], ones[:, :], wg_sb[:, :, :].rearrange("p k e -> p (k e)"),
                             start=True, stop=True).then_inc(mean_ready, 1)
            pe.wait_ge(wj_ready, 1)

            def context(c, r):
                pe.wait_ge(ctx_landed[r], 16 * ((c - r) // RING + 1))
                for d in range(DC):
                    last = nc.tensor.transpose(ctx_ps[:, P * d:P * (d + 1)], ctx_in[:, r, P * d:P * (d + 1)],
                                               ident[:, :])
                last.then_inc(ctx_turned, 1)
                pe.wait_ge(ctx_copied, c + 1)
                for d in range(DC):
                    nc.tensor.matmul(sj_ps[:, 0:P], wj_bc[:, d, :], ctx_tr[:, r % 2, d, :],
                                     start=(d == 0), stop=(d == DC - 1))
                for d in range(DC):
                    last = nc.tensor.matmul(sj_ps[:, P:P + 1], ctx_tr[:, r % 2, d, :], wcol[:, d:d + 1],
                                            start=(d == 0), stop=(d == DC - 1))
                last.then_inc(sj_summed, 1)

            with pe.Fori(0, TB // RING) as i:
                for r in range(RING):
                    pe.wait_ge(sj_ready, RING * i + r)
                    context(RING * i + r, r)
            pe.wait_ge(wgc_ready, 1)

            def tiles(i, more_ctx):
                for r in range(RING):
                    t = RING * i + r
                    if more_ctx:
                        pe.wait_ge(sj_ready, t + TB)
                        context(t + TB, r)
                    pe.wait_ge(x1_ready, t + 1)
                    for g in range(2):
                        for k in range(KH):
                            last = nc.tensor.transpose(xt_ps[g][:, P * k:P * (k + 1)],
                                                       x1[:, r, P * (KH * g + k):P * (KH * g + k + 1)], ident[:, :])
                        last.then_inc(x1_turned, 1)
                    pe.wait_ge(x1_copied, 2 * t + 2)
                    for k in range(K):
                        last = nc.tensor.matmul(lg_ps[:, bass.ds(E * t, E)], x1_tr[:, k, :], wg_c[:, k, :],
                                                start=(k == 0), stop=(k == K - 1))
                    last.then_inc(logits_ready, 1)

            with pe.Fori(0, MAIN) as i:
                tiles(i, True)
            for i in range(MAIN, LAST + 1):
                tiles(i, False)

            pe.wait_ge(onehot_ready, 1)
            hot = onehot[:, :, :].rearrange("p t e -> p (t e)")
            nc.tensor.matmul(rank_ps[:, 0:T * E], before[:, :], hot, start=True, stop=True)
            nc.tensor.matmul(total_ps[:, 0:T * E], ones[:, :], hot, start=True, stop=True).then_inc(ranks_ready, 1)

            def weight_group(e, g):
                j, kh = g // 2, g % 2
                if kh == 0:
                    pe.wait_ge(w_landed[j], 16 * e + 16)
                for k in range(KH):
                    c = KH * kh + k
                    last = nc.tensor.transpose(w_ps[g % WP][:, P * k:P * (k + 1)], w_raw[:, j, P * c:P * (c + 1)],
                                               ident[:, :])
                last.then_inc(w_turned, 1)

            pe.wait_ge(hot_ready, 1)
            for t in range(T):
                last = nc.tensor.matmul(meta_ps[:, 0:META * TAB], lane_hot[:, t, :],
                                        slot_val[:, t, :, :].rearrange("p m s -> p (m s)"),
                                        start=(t == 0), stop=(t == T - 1))
            last.then_inc(meta_ready, 1)
            for g in range(G):
                if g == WP - 1:
                    pe.wait_ge(route_ready, 1)
                if g >= WP:
                    pe.wait_ge(w_lo_ready, g - WP + 1)
                weight_group(0, g)

            def turn(t):
                pe.wait_ge(xn_ready, t + 1)
                for g in range(2):
                    for k in range(KH):
                        last = nc.tensor.transpose(xt_ps[g][:, P * k:P * (k + 1)],
                                                   xn[:, P * (KH * g + k):P * (KH * g + k + 1)], ident[:, :])
                    last.then_inc(xt_turned[g], 1)

            def multiply(t, e, par, prepare):
                pe.wait_ge(w_lo_ready, G * e + G)
                for h in range(2):
                    pe.wait_ge(res_ready[h], t)
                    if h == 1:
                        turn(t + 1)
                    for k in range(K):
                        if h == 0 and k % KH == 0:
                            pe.wait_ge(xt_ready[k // KH], t + 1)
                        for n, (xs, part) in enumerate(((xt_hi, 0), (xt_hi, 1), (xt_lo, 0))):
                            last = nc.tensor.matmul(
                                out_ps[h][:, :], xs[:, k, :],
                                wt[:, bass.ds(par, 1), part, k, HALF * h:HALF * (h + 1)]
                                .rearrange("p a o -> p (a o)"),
                                start=(k == 0 and n == 0), stop=(k == K - 1 and n == 2))
                        if k == K - 1:
                            last.then_inc(sum_ready[h], 1)
                        if h == 1 and k == KH - 1:
                            last.then_inc(xt_used, 1)
                        if prepare:
                            g = K * h + k
                            pe.wait_ge(w_lo_ready, G * (e + 1) + g - WP + 1)
                            weight_group(e + 1, g)

            pe.wait_ge(route_ready, 1)
            turn(0)
            with pe.Fori(0, SLOTS) as t:
                kind = pe.value_load(slot_tab[0:1, 0, bass.ds(t, 1)], min_val=0, max_val=2)
                e = pe.value_load(slot_tab[0:1, 1, bass.ds(t, 1)], min_val=0, max_val=E - 1)
                par = pe.snap(e % 2)
                with pe.If(kind > 1):
                    multiply(t, e, par, True)
                with pe.Else():
                    with pe.If(kind > 0):
                        multiply(t, e, par, False)
                    with pe.Else():
                        pe.nop()
                    pe.nop()


def kernel(**inputs):
    import concourse.bacc as bacc
    from concourse.bass_utils import run_bass_kernel_spmd

    names = ["x", "ctx_512", "g_xattn", "g_ffn", "L0_xattn_W", "L0_xattn_b", "L0_ffn_wg", "L0_ffn_W", "L0_ffn_b"]
    nc = bacc.Bacc("TRN2", target_bir_lowering=False, num_devices=1)
    arrays, args = {}, []
    for name in names:
        a = np.ascontiguousarray(inputs[name])
        arrays[f"in_{name}"] = a
        args.append(nc.dram_tensor(f"in_{name}", a.shape, mybir.dt.from_np(a.dtype), kind="ExternalInput").ap())
    shape = inputs["x"].shape
    args.append(nc.dram_tensor("out_x", shape, F32, kind="ExternalOutput").ap())
    build(nc, *args)
    r = run_bass_kernel_spmd(nc, [arrays], core_ids=[0])
    return r.results[0]["out_x"]
```
